# Optimizing a Trainium2 kernel written in Bass

```python
import numpy as np
import jax
import jax.numpy as jnp

def _softmax(x, axis=-1):
    return jax.nn.softmax(x, axis=axis)

def _gelu(x):
    return jax.nn.gelu(x, approximate=True)

def _silu(x):
    return jax.nn.silu(x)

def _sigmoid(x):
    return jax.nn.sigmoid(x)

def _layernorm(x, axis=-1, eps=1e-05):
    m = jnp.mean(x, axis=axis, keepdims=True)
    v = jnp.var(x, axis=axis, keepdims=True)
    return (x - m) / jnp.sqrt(v + eps)

def _scatter_add(tgt, idx, src, axis=0):
    return tgt.at[idx].add(src)

def _segment_sum(src, seg, n):
    return jax.ops.segment_sum(src, seg, n)
kernel_name = 'mk_gnn_resnorm_d2_gnn_r8_2e002e'

def setup_inputs(seed: int=0):
    np.random.seed(seed)
    _w = jnp.asarray

    def _rec_inputs():
        import jax
        import jax.numpy as jnp
        _gk = jax.random.key(seed)
        x = -0.000202 + 1 * jax.random.normal(jax.random.fold_in(_gk, 1), (12500, 64), jnp.float32)
        src = jax.random.randint(jax.random.fold_in(_gk, 2), (200000,), 0, 12500, jnp.int32)
        dst = jax.random.randint(jax.random.fold_in(_gk, 3), (200000,), 0, 12500, jnp.int32)
        _o = jnp.argsort(dst, stable=True)
        src = src[_o]
        dst = dst[_o]
        edge_attr_64 = 7.68618e-05 + 1.00005 * jax.random.normal(jax.random.fold_in(_gk, 12), (200000, 64), jnp.float32)
        edge_weight1 = -0.000414295 + 0.999828 * jax.random.normal(jax.random.fold_in(_gk, 14), (200000, 1), jnp.float32)
        return (x, src, dst, edge_attr_64, edge_weight1)
    x, src, dst, edge_attr_64, edge_weight1 = _rec_inputs()

    def _L0_gnn_setup():
        import jax, jax.numpy as jnp
        import numpy as np
        N_NODES = 12500
        N_EDGES = 125000
        D_IN = 64
        D_OUT = 64
        key = jax.random.key(seed)
        k_x, k_ei, k_ea, k_w, k_b = jax.random.split(key, 5)
        x = jax.random.normal(k_x, (N_NODES, D_IN), dtype=jnp.float32)
        edge_index = jax.random.randint(k_ei, (2, N_EDGES), 0, N_NODES, dtype=jnp.int64)
        edge_attr = jax.random.normal(k_ea, (N_EDGES, D_IN), dtype=jnp.float32)
        bound = 1.0 / np.sqrt(D_IN)
        W = jax.random.uniform(k_w, (D_OUT, D_IN), dtype=jnp.float32, minval=-bound, maxval=bound)
        b = jax.random.uniform(k_b, (D_OUT,), dtype=jnp.float32, minval=-bound, maxval=bound)
        eps = jnp.zeros((), dtype=jnp.float32)
        return {'x': x, 'edge_index': edge_index, 'edge_attr': edge_attr, 'W': W, 'b': b, 'eps': eps}
    _L0_gnn_all = _L0_gnn_setup()
    _L0_gnn_in = {k: v for k, v in _L0_gnn_all.items() if k in ('W', 'b', 'eps')}
    del _L0_gnn_all

    def _L1_gnn_setup():
        import jax, jax.numpy as jnp
        import numpy as np
        N_NODES = 12500
        N_EDGES = 200000
        IN_FEATS = 64
        OUT_FEATS = 64
        EDGE_FEATS = 1
        key = jax.random.key(seed)
        ks = jax.random.split(key, 6)
        h = jax.random.normal(ks[0], (N_NODES, IN_FEATS), dtype=jnp.float32)
        e = jax.random.normal(ks[1], (N_EDGES, EDGE_FEATS), dtype=jnp.float32)
        src = jax.random.randint(ks[2], (N_EDGES,), 0, N_NODES, dtype=jnp.int32)
        dst = jax.random.randint(ks[3], (N_EDGES,), 0, N_NODES, dtype=jnp.int32)
        cat_dim = 2 * IN_FEATS + EDGE_FEATS
        W1 = jax.random.normal(ks[4], (cat_dim, OUT_FEATS), dtype=jnp.float32) / np.sqrt(cat_dim)
        b1 = jnp.zeros((OUT_FEATS,), dtype=jnp.float32)
        W2 = jax.random.normal(ks[5], (OUT_FEATS, OUT_FEATS), dtype=jnp.float32) / np.sqrt(OUT_FEATS)
        b2 = jnp.zeros((OUT_FEATS,), dtype=jnp.float32)
        return {'h': h, 'e': e, 'src': src, 'dst': dst, 'W1': W1, 'b1': b1, 'W2': W2, 'b2': b2}
    _L1_gnn_all = _L1_gnn_setup()
    _L1_gnn_in = {k: v for k, v in _L1_gnn_all.items() if k in ('W1', 'b1', 'W2', 'b2')}
    del _L1_gnn_all
    return {'x': x, 'src': src, 'dst': dst, 'edge_attr_64': edge_attr_64, 'edge_weight1': edge_weight1, 'L0_gnn_W': _L0_gnn_in['W'], 'L0_gnn_b': _L0_gnn_in['b'], 'L0_gnn_eps': _L0_gnn_in['eps'], 'L1_gnn_W1': _L1_gnn_in['W1'], 'L1_gnn_b1': _L1_gnn_in['b1'], 'L1_gnn_W2': _L1_gnn_in['W2'], 'L1_gnn_b2': _L1_gnn_in['b2']}

def reference(x, src, dst, edge_attr_64, edge_weight1, L0_gnn_W, L0_gnn_b, L0_gnn_eps, L1_gnn_W1, L1_gnn_b1, L1_gnn_W2, L1_gnn_b2):
    import jax
    import jax.numpy as jnp

    def _L0_gnn_ref(x, edge_index, edge_attr, W, b, eps):
        import jax, jax.numpy as jnp
        import numpy as np
        N_NODES = 12500
        N_EDGES = 125000
        D_IN = 64
        D_OUT = 64
        src = edge_index[0]
        dst = edge_index[1]
        msg = jax.nn.relu(x[src] + edge_attr)
        agg = jax.ops.segment_sum(msg, dst, num_segments=x.shape[0])
        h = (1.0 + eps) * x + agg
        out = h @ W.T + b
        return jax.nn.relu(out)

    def _L1_gnn_ref(h, e, src, dst, W1, b1, W2, b2):
        import jax, jax.numpy as jnp
        import numpy as np
        N_NODES = 12500
        N_EDGES = 200000
        IN_FEATS = 64
        OUT_FEATS = 64
        EDGE_FEATS = 1
        x = jnp.concatenate([h[src], h[dst], e], axis=1)
        m = jax.nn.relu(x @ W1 + b1) @ W2 + b2
        h_new = jax.ops.segment_sum(m, dst, num_segments=h.shape[0])
        return h_new
    edge_index = jnp.stack([src, dst])
    x = _layernorm(x + _L0_gnn_ref(x, edge_index, edge_attr_64, L0_gnn_W, L0_gnn_b, L0_gnn_eps), axis=-1)
    x = _layernorm(x + _L1_gnn_ref(x, edge_weight1, src, dst, L1_gnn_W1, L1_gnn_b1, L1_gnn_W2, L1_gnn_b2), axis=-1)
    return x

_drawn_inputs = setup_inputs


def setup_inputs(seed=0):
    import zlib

    import numpy as np

    out = dict(_drawn_inputs(seed))
    spreads = {'L1_gnn_b1': (0.0, 0.1), 'L1_gnn_b2': (0.0, 0.1)}
    factors = {'L0_gnn_b': 4.891, 'edge_weight1': 2.692}
    for name, (base, spread) in spreads.items():
        noise = np.random.default_rng([zlib.crc32(name.encode()), seed]).standard_normal(out[name].shape)
        drawn = base * np.exp(spread * noise) if base else spread * noise
        out[name] = jnp.asarray(drawn.astype(out[name].dtype))
    for name, factor in factors.items():
        out[name] = (out[name] * factor).astype(out[name].dtype)
    return out
```

```python
from contextlib import ExitStack

import concourse.bass as bass
from concourse import mybir

F32 = mybir.dt.float32
I32 = mybir.dt.int32
ALU = mybir.AluOpType
ACT = mybir.ActivationFunctionType
AX = mybir.AxisListType

P = 128
D = 64
N = 12500
E = 200000
TILES = 8
GROUP = P * TILES
RING = 4
TURNS = -(-E // (GROUP * RING))
GROUPS = TURNS * RING
E_PAD = GROUPS * GROUP
WIN = 128
BLK = 7
BATCH = P * BLK
BATCHES = -(-N // BATCH)
N_PAD = BATCHES * BATCH
COLS = N_PAD + WIN
HALF = GROUPS // 2
LN_EPS = 1e-5
BANK = 4
assert BATCHES % 2 == 0 and HALF <= P and N < N_PAD


def two_back(u, m):
    return (u - 2, m + 1) if u >= 2 else (u + 2, m)


def build(nc, x, src, dst, ea, ew, W, b, eps, W1, b1, W2, b2, out):
    ctx = ExitStack()
    with ctx:
        def sb(name, shape, dt=F32):
            return ctx.enter_context(nc.sbuf_tensor(name, shape, dt))

        def ps(name, cols):
            return ctx.enter_context(nc.psum_tensor(name, [P, cols], F32))

        def sem(name):
            return ctx.enter_context(nc.semaphore(name))

        def ring_sem(name):
            return [sem(f"{name}{u}") for u in range(RING)]

        def pair_sem(name):
            return [sem(f"{name}{u}") for u in range(2)]

        A_dram = nc.dram_tensor("A_dram", (N_PAD, D), F32).ap()
        B_dram = nc.dram_tensor("B_dram", (COLS, D), F32).ap()
        x1_dram = nc.dram_tensor("x1_dram", (N_PAD, D), F32).ap()

        ident = sb("ident", [P, P])
        iota_i = sb("iota_i", [P, WIN], I32)
        window = sb("window", [P, WIN])
        ones = sb("ones", [P, P])
        zeros = sb("zeros", [P, BATCH])
        W_in = sb("W_in", [D, D])
        WT65 = sb("WT65", [D + 1, D])
        W1AB = sb("W1AB", [D + 1, 2 * D])
        W2_65 = sb("W2_65", [D + 1, D])
        w_edge = sb("w_edge", [P, D])
        eps_in = sb("eps_in", [D, 1])
        one_eps = sb("one_eps", [D, 1])
        ln_eps = sb("ln_eps", [P, 1])

        dst_i = sb("dst_i", [P, GROUPS, TILES], I32)
        dst_rel = sb("dst_rel", [P, GROUPS, TILES])
        low_p = sb("low_p", [P, GROUPS])
        high_p = sb("high_p", [P, GROUPS])
        low_g = sb("low_g", [HALF, 2])
        high_g = sb("high_g", [HALF, 2])
        diag = sb("diag", [HALF, 4, HALF])
        low_all = sb("low_all", [P, GROUPS])
        span = sb("span", [P, GROUPS])
        span_max = sb("span_max", [P, 1])
        low_i = sb("low_i", [P, GROUPS], I32)
        span_i = sb("span_i", [P, 1], I32)

        sum0 = sb("sum0", [D + 1, COLS])
        sum1 = sb("sum1", [D + 1, COLS])

        idx = sb("idx", [P, RING, TILES], I32)
        attr = sb("attr", [P, RING, TILES * D])
        gat = sb("gat", [P, RING, TILES * D])
        msg = sb("msg", [P, RING, TILES, D + 1])
        hot = sb("hot", [P, RING, TILES, WIN])
        hotT = sb("hotT", [P, 2, TILES, P])
        ew_in = sb("ew_in", [P, RING, TILES])
        edge_term = sb("edge_term", [P, 2, TILES, D])
        B_win = sb("B_win", [WIN, RING, D])

        x_b = sb("x_b", [P, 2, BLK * D])
        hT = sb("hT", [D + 1, 2, BLK, P])
        y = sb("y", [P, 2, BLK, D])
        stats = sb("stats", [P, 2, BLK, 6])
        mean_var = sb("mean_var", [P, 2, BLK, 2])
        std = sb("std", [P, 2, BLK])
        rstd = sb("rstd", [P, 2, BLK])
        x1_b = sb("x1_b", [P, 2, BLK, D])
        x1T = sb("x1T", [D + 1, 2, BLK, P])
        A_b = attr[:, 0:2, 0:BLK * D].rearrange("p w (c d) -> p w c d", d=D)
        B_b = attr[:, 2:4, 0:BLK * D].rearrange("p w (c d) -> p w c d", d=D)

        sum_ps = [ps(f"sum_ps{w}", 512) for w in range(2)]
        z_ps = [ps(f"z_ps{w}", 512) for w in range(2)]
        wide_ps = [ps(f"wide_ps{w}", 1024) for w in range(2)]

        waits_carried = sem("waits_carried")
        weights_in = sem("weights_in")
        dst_in = sem("dst_in")
        ident_made = sem("ident_made")
        dve_setup = sem("dve_setup")
        pe_setup = sem("pe_setup")
        pads_done = sem("pads_done")
        windows_known = sem("windows_known")
        window_moved = sem("window_moved")
        x_in = pair_sem("x_in")
        x_turned = pair_sem("x_turned")
        x_scaled = pair_sem("x_scaled")
        idx_in = ring_sem("idx_in")
        attr_in = ring_sem("attr_in")
        gathered = ring_sem("gathered")
        hot_made = ring_sem("hot_made")
        added = ring_sem("added")
        msg_made = ring_sem("msg_made")
        seg_done = ring_sem("seg_done")
        sum_kept = ring_sem("sum_kept")
        idx_in1 = ring_sem("idx1_in")
        ew_in1 = ring_sem("ew1_in")
        B_in1 = ring_sem("B1_in")
        gathered1 = ring_sem("gathered1_")
        hot_made1 = ring_sem("hot1_made")
        turned1 = ring_sem("turned1_")
        hotT_made1 = ring_sem("hotT1_made")
        spread1 = ring_sem("spread1_")
        edge_term1 = ring_sem("edge_term1_")
        part_added1 = ring_sem("part_added1_")
        added1 = ring_sem("added1_")
        msg_made1 = ring_sem("msg1_made")
        seg_done1 = ring_sem("seg1_done")
        sum_kept1 = ring_sem("sum1_kept")
        res_in = [pair_sem("res0_in"), pair_sem("res1_in")]
        hT_made = [pair_sem("hT0_made"), pair_sem("hT1_made")]
        proj_done = [pair_sem("proj0_done"), pair_sem("proj1_done")]
        y_made = [pair_sem("y0_made"), pair_sem("y1_made")]
        stats_made = [pair_sem("stats0_made"), pair_sem("stats1_made")]
        var_made = [pair_sem("var0_made"), pair_sem("var1_made")]
        std_made = [pair_sem("std0_made"), pair_sem("std1_made")]
        rstd_made = [pair_sem("rstd0_made"), pair_sem("rstd1_made")]
        norm_made = [pair_sem("norm0_made"), pair_sem("norm1_made")]
        norm_out = [pair_sem("norm0_out"), pair_sem("norm1_out")]
        x1_turned = pair_sem("x1_turned")
        x1T_made = pair_sem("x1T_made")
        AB_done = pair_sem("AB_done")
        AB_copied = pair_sem("AB_copied")
        A_out = pair_sem("A_out")
        B_out = pair_sem("B_out")

        dst_v = dst.rearrange("(g p j) -> p g j", p=P, j=TILES)

        def edges(t, u):
            return (t * RING + u) * GROUP

        def src_v(t, u):
            return src[bass.ds(edges(t, u), GROUP)].rearrange("(p j) -> p j", p=P)

        def ea_v(t, u):
            return ea[bass.ds(edges(t, u), GROUP), :].rearrange("(p j) d -> p (j d)", p=P)

        def ew_v(t, u):
            return ew[bass.ds(edges(t, u), GROUP), :].rearrange("(p j) o -> p (j o)", p=P)

        def batch_v(dram, s):
            return dram[bass.ds(s * BATCH, BATCH), :].rearrange("(p c) d -> p (c d)", p=P)

        def cols_v(sums, s):
            return sums[:, bass.ds(s * BATCH, BATCH)].rearrange("k (p c) -> k c p", p=P)

        def passes(eng):
            eng.wait_ge(windows_known, 1)
            return eng.snap((eng.value_load(span_i[0:1, 0:1], min_val=0, max_val=N_PAD - 1) >> 7) + 1,
                            min_val=1, max_val=COLS // WIN)

        def window_start(eng, k, t, u):
            low = eng.value_load(low_i[0:1, bass.ds(t * RING + u, 1)], min_val=0, max_val=N_PAD - 1)
            start = start_regs[eng.engine]
            eng.reg_mov(start, low + k * WIN)
            eng.reg_alu(start, start, N_PAD, op=ALU.min)
            return eng.snap(start, min_val=0, max_val=N_PAD)

        start_regs = {eng.engine: eng.alloc_register("window_start") for eng in (nc.sync, nc.vector)}

        def carry_wait(eng):
            eng.sem_inc(waits_carried, 1)

        block = ctx.enter_context(nc.Block())

        @block.sync
        def _(sp):
            sp.dma_start(dst_i[:], dst_v).then_inc(dst_in, 16)

            def load_group0(t, m, u):
                sp.wait_ge(gathered[u], m * (16 * TILES))
                sp.dma_start(idx[:, u, :], src_v(t, u)).then_inc(idx_in[u], 16)
                sp.wait_ge(added[u], m)
                sp.dma_start(attr[:, u, :], ea_v(t, u)).then_inc(attr_in[u], 16)

            for u in range(RING):
                load_group0(0, 0, u)

            sp.dma_start(x_b[:, 0, :], batch_v(x, 0)).then_inc(x_in[0], 16)
            sp.dma_start(x_b[:, 1, :], batch_v(x, 1)).then_inc(x_in[1], 16)
            sp.dma_start(eps_in[:], eps.to_broadcast([D, 1])).then_inc(weights_in, 16)
            sp.dma_start(W_in[:], W).then_inc(weights_in, 16)
            sp.dma_start(WT65[D:D + 1, :], b).then_inc(weights_in, 16)
            sp.dma_start(W1AB[0:D, 0:D], W1[0:D, :]).then_inc(weights_in, 16)
            sp.dma_start(W1AB[0:D, D:2 * D], W1[D:2 * D, :]).then_inc(weights_in, 16)
            sp.dma_start(W1AB[D:D + 1, 0:D], b1).then_inc(weights_in, 16)
            sp.dma_start(W2_65[0:D, :], W2).then_inc(weights_in, 16)
            sp.dma_start(W2_65[D:D + 1, :], b2).then_inc(weights_in, 16)
            sp.dma_start(w_edge[:], W1[2 * D:2 * D + 1, :].to_broadcast([P, D])).then_inc(weights_in, 16)
            sp.wait_ge(dve_setup, 1)
            sp.dma_start(W1AB[D:D + 1, D:2 * D], zeros[0:1, 0:D]).then_inc(pads_done, 16)
            sp.dma_start(sum0[0:D, N_PAD:COLS], zeros[0:D, 0:WIN]).then_inc(pads_done, 16)
            sp.dma_start(sum1[:, N_PAD:COLS], zeros[0:D + 1, 0:WIN]).then_inc(pads_done, 16)
            sp.dma_start(B_dram[N_PAD:COLS, :], zeros[:, 0:D]).then_inc(pads_done, 16)
            with sp.Fori(1, BATCHES // 2) as i:
                for w in range(2):
                    sp.wait_ge(x_turned[w], i)
                    sp.dma_start(x_b[:, w, :], batch_v(x, i * 2 + w)).then_inc(x_in[w], 16)
            with sp.Fori(0, BATCHES) as i:
                sp.dma_start(sum1[:, bass.ds(i * BATCH, BATCH)], zeros[0:D + 1, :]).then_inc(pads_done, 16)

            with sp.Fori(1, TURNS) as t:
                for u in range(RING):
                    load_group0(t, t, u)
            n_pass = passes(sp)
            with sp.If(n_pass > 1):
                with sp.Fori(1, n_pass) as k:
                    with sp.Fori(0, TURNS) as t:
                        for u in range(RING):
                            load_group0(t, k * TURNS + t, u)

            def load_residual(ph, s, i, w, dram):
                sp.wait_ge(y_made[ph][w], i)
                sp.dma_start(x_b[:, w, :], batch_v(dram, s)).then_inc(res_in[ph][w], 16)

            for w in range(2):
                sp.wait_ge(x_turned[w], BATCHES // 2)
            with sp.Fori(0, BATCHES // 2) as i:
                for w in range(2):
                    load_residual(0, i * 2 + w, i, w, x)
                for w in range(2):
                    sp.wait_ge(norm_made[0][w], i + 1)
                    sp.dma_start(batch_v(x1_dram, i * 2 + w), x1_b[:, w].rearrange("p c d -> p (c d)")
                                 ).then_inc(norm_out[0][w], 16)
                    sp.wait_ge(AB_copied[w], i + 1)
                    sp.dma_start(batch_v(A_dram, i * 2 + w), attr[:, w, 0:BLK * D]
                                 ).then_inc(A_out[w], 16)
                    sp.dma_start(batch_v(B_dram, i * 2 + w), attr[:, 2 + w, 0:BLK * D]
                                 ).then_inc(B_out[w], 16)

            sp.wait_ge(pads_done, 16 * (4 + BATCHES))
            for w in range(2):
                sp.wait_ge(B_out[w], 16 * (BATCHES // 2))
                sp.wait_ge(norm_out[0][w], 16 * (BATCHES // 2))
            n_pass1 = passes(sp)
            with sp.Fori(0, n_pass1) as k:
                with sp.Fori(0, TURNS) as t:
                    m = sp.snap(k * TURNS + t)
                    for u in range(RING):
                        sp.wait_ge(gathered1[u], m * (16 * TILES))
                        sp.dma_start(idx[:, u, :], src_v(t, u)).then_inc(idx_in1[u], 16)
                        sp.wait_ge(edge_term1[u], m)
                        sp.dma_start(ew_in[:, u, :], ew_v(t, u)).then_inc(ew_in1[u], 16)
                        sp.wait_ge(spread1[u], m)
                        start = window_start(sp, k, t, u)
                        sp.dma_start(B_win[:, u, :], B_dram[bass.ds(start, WIN), :]).then_inc(B_in1[u], 16)

            with sp.Fori(0, BATCHES // 2) as i:
                for w in range(2):
                    load_residual(1, i * 2 + w, i, w, x1_dram)
                for w in range(2):
                    sp.wait_ge(norm_made[1][w], i + 1)
                    sp.dma_start(batch_v(out, i * 2 + w), x1_b[:, w].rearrange("p c d -> p (c d)")
                                 ).then_inc(norm_out[1][w], 16)
            for w in range(2):
                sp.wait_ge(norm_out[1][w], 16 * (BATCHES // 2))
                sp.wait_ge(A_out[w], 16 * (BATCHES // 2))

        @block.gpsimd
        def _(pool):
            pool.memset(ident[:], 0.0).then_inc(ident_made, 1)
            pool.iota(iota_i[:], pattern=[[1, WIN]], base=0, channel_multiplier=0).then_inc(ident_made, 1)
            pool.wait_ge(ident_made, 2)
            pool.affine_select(out=ident[:], in_=ident[:], compare_op=ALU.not_equal, fill=1.0, base=0,
                               pattern=[[-1, P]], channel_multiplier=1).then_inc(ident_made, 1)

            def gather_group(table, u, m, idx_sem, free_sem, done_sem):
                pool.wait_ge(idx_sem[u], (m + 1) * 16)
                pool.wait_ge(free_sem[u], m)
                carry_wait(pool)
                for j in range(TILES):
                    pool.indirect_dma_start(
                        out=gat[:, u, j * D:(j + 1) * D], out_offset=None, in_=table[:, :],
                        in_offset=bass.IndirectOffsetOnAxis(ap=idx[:, u, j:j + 1], axis=0),
                    ).then_inc(done_sem[u], 16)

            def gather_pass(table, k, idx_sem, free_sem, done_sem):
                with pool.Fori(0, TURNS) as t:
                    m = pool.snap(k * TURNS + t)
                    for u in range(RING):
                        gather_group(table, u, m, idx_sem, free_sem, done_sem)

            gather_pass(x, 0, idx_in, msg_made, gathered)
            n_pass = passes(pool)
            with pool.If(n_pass > 1):
                with pool.Fori(1, n_pass) as k:
                    gather_pass(x, k, idx_in, msg_made, gathered)
            for w in range(2):
                pool.wait_ge(A_out[w], 16 * (BATCHES // 2))
            with pool.Fori(0, n_pass) as k:
                gather_pass(A_dram, k, idx_in1, msg_made1, gathered1)

        @block.scalar
        def _(act):
            act.wait_ge(dve_setup, 2)
            with act.Fori(0, BATCHES // 2) as i:
                for w in range(2):
                    act.wait_ge(x_turned[w], i + 1)
                    act.activation(cols_v(sum0, i * 2 + w)[0:D],
                                   wide_ps[w][0:D, 0:BATCH].rearrange("k (c p) -> k c p", p=P),
                                   ACT.Copy, scale=one_eps[:, 0:1]).then_inc(x_scaled[w], 1)

            n_pass = passes(act)
            with act.Fori(0, n_pass) as k:
                with act.Fori(0, TURNS) as t:
                    m = act.snap(k * TURNS + t)
                    for u in range(RING):
                        act.wait_ge(added[u], m + 1)
                        act.wait_ge(seg_done[u], m)
                        act.activation(msg[:, u, :, 0:D], gat[:, u, :].rearrange("p (j d) -> p j d", d=D),
                                       ACT.Relu).then_inc(msg_made[u], 1)

            def turn_sums(ph, sums, s, i, w):
                act.wait_ge(proj_done[ph][w], i)
                act.activation(hT[:, w], cols_v(sums, s), ACT.Copy).then_inc(hT_made[ph][w], 1)

            def root(ph, i, w):
                act.wait_ge(var_made[ph][w], i + 1)
                act.activation(std[:, w, :], mean_var[:, w, :, 1], ACT.Sqrt, bias=ln_eps[:, 0:1]
                               ).then_inc(std_made[ph][w], 1)

            for u in range(RING):
                act.wait_ge(sum_kept[u], n_pass * TURNS)
            with act.Fori(0, BATCHES // 2) as i:
                for w in range(2):
                    turn_sums(0, sum0, i * 2 + w, i, w)
                for w in range(2):
                    root(0, i, w)
                for w in range(2):
                    act.wait_ge(x1_turned[w], i + 1)
                    act.wait_ge(AB_done[w], i)
                    act.activation(x1T[0:D, w], wide_ps[w][0:D, 0:BATCH].rearrange("k (c p) -> k c p", p=P),
                                   ACT.Copy).then_inc(x1T_made[w], 1)
                for w in range(2):
                    act.wait_ge(AB_done[w], i + 1)
                    act.wait_ge(A_out[w], i * 16)
                    act.wait_ge(B_out[w], i * 16)
                    AB = wide_ps[w][:, 0:BATCH].rearrange("p (c d) -> p c d", d=2 * D)
                    act.activation(A_b[:, w], AB[:, :, 0:D], ACT.Copy)
                    act.activation(B_b[:, w], AB[:, :, D:2 * D], ACT.Copy).then_inc(AB_copied[w], 1)

            def copy_turned(m, u):
                w = u % 2
                act.wait_ge(turned1[u], m + 1)
                v, c = two_back(u, m)
                act.wait_ge(spread1[v], c)
                for h in range(2):
                    act.activation(hotT[:, w, h * BANK:(h + 1) * BANK, :],
                                   wide_ps[w][:, h * 512:(h + 1) * 512].rearrange("p (j q) -> p j q", q=P),
                                   ACT.Copy).then_inc(hotT_made1[u], 1)

            def relu1(m, u):
                act.wait_ge(added1[u], m + 1)
                act.wait_ge(seg_done1[u], m)
                act.activation(msg[:, u, :, 0:D], gat[:, u, :].rearrange("p (j d) -> p j d", d=D),
                               ACT.Relu).then_inc(msg_made1[u], 1)

            with act.Fori(0, n_pass) as k:
                with act.Fori(0, TURNS) as t:
                    m = act.snap(k * TURNS + t)
                    copy_turned(m, 0)
                    for u in range(RING):
                        if u + 1 < RING:
                            copy_turned(m, u + 1)
                        relu1(m, u)

            for u in range(RING):
                act.wait_ge(sum_kept1[u], n_pass * TURNS)
            with act.Fori(0, BATCHES // 2) as i:
                for w in range(2):
                    turn_sums(1, sum1, i * 2 + w, i, w)
                for w in range(2):
                    root(1, i, w)

        @block.tensor
        def _(pe):
            pe.wait_ge(ident_made, 3)
            pe.wait_ge(dve_setup, 3)
            for h in range(2):
                pe.transpose(sum_ps[h][0:HALF, 0:P], low_p[:, h * HALF:(h + 1) * HALF], ident[:])
                mm = pe.transpose(z_ps[h][0:HALF, 0:P], high_p[:, h * HALF:(h + 1) * HALF], ident[:])
            mm.then_inc(pe_setup, 1)
            pe.wait_ge(weights_in, 16 * 9)
            pe.transpose(wide_ps[0][0:D, 0:D], W_in[:], ident[0:D, 0:D]).then_inc(pe_setup, 1)
            pe.wait_ge(dve_setup, 5)
            for h in range(2):
                pe.matmul(sum_ps[h][:, 0:HALF], ones[0:HALF, :], diag[:, h, :], start=True, stop=True)
                mm = pe.matmul(z_ps[h][:, 0:HALF], ones[0:HALF, :], diag[:, 2 + h, :], start=True, stop=True)
            mm.then_inc(pe_setup, 1)
            pe.wait_ge(dve_setup, 6)
            with pe.Fori(0, BATCHES // 2) as i:
                for w in range(2):
                    pe.wait_ge(x_in[w], (i + 1) * 16)
                    pe.wait_ge(x_scaled[w], i)
                    carry_wait(pe)
                    for c in range(BLK):
                        mm = pe.transpose(wide_ps[w][0:D, c * P:(c + 1) * P], x_b[:, w, c * D:(c + 1) * D], ident[:])
                    mm.then_inc(x_turned[w], 1)

            def segment_sums(m, u, rows, msg_sem, hot_sem, kept_sem, done_sem):
                pe.wait_ge(msg_sem[u], m + 1)
                pe.wait_ge(hot_sem[u], m + 1)
                v, c = two_back(u, m)
                pe.wait_ge(kept_sem[v], c)
                for j in range(TILES):
                    mm = pe.matmul(sum_ps[u % 2][0:rows, 0:WIN], msg[:, u, j, 0:rows], hot[:, u, j, :],
                                   start=(j == 0), stop=(j == TILES - 1))
                mm.then_inc(done_sem[u], 1)

            n_pass = passes(pe)
            with pe.Fori(0, n_pass) as k:
                with pe.Fori(0, TURNS) as t:
                    m = pe.snap(k * TURNS + t)
                    for u in range(RING):
                        segment_sums(m, u, D, msg_made, hot_made, sum_kept, seg_done)

            def project(ph, i, w, weights):
                pe.wait_ge(hT_made[ph][w], i + 1)
                pe.wait_ge(y_made[ph][w], i)
                for c in range(BLK):
                    mm = pe.matmul(z_ps[w][:, c * D:(c + 1) * D], hT[:, w, c, :], weights[:],
                                   start=True, stop=True)
                mm.then_inc(proj_done[ph][w], 1)

            with pe.Fori(0, BATCHES // 2) as i:
                for w in range(2):
                    project(0, i, w, WT65)
                for w in range(2):
                    pe.wait_ge(norm_made[0][w], i + 1)
                    pe.wait_ge(AB_copied[w], i)
                    carry_wait(pe)
                    for c in range(BLK):
                        mm = pe.transpose(wide_ps[w][0:D, c * P:(c + 1) * P], x1_b[:, w, c, :], ident[:])
                    mm.then_inc(x1_turned[w], 1)
                for w in range(2):
                    pe.wait_ge(x1T_made[w], i + 1)
                    for c in range(BLK):
                        mm = pe.matmul(wide_ps[w][:, c * P:(c + 1) * P], x1T[:, w, c, :], W1AB[:],
                                       start=True, stop=True)
                    mm.then_inc(AB_done[w], 1)

            def turn_hot(m, u):
                pe.wait_ge(hot_made1[u], m + 1)
                v, c = two_back(u, m)
                pe.wait_ge(hotT_made1[v], c * 2)
                for j in range(TILES):
                    mm = pe.transpose(wide_ps[u % 2][:, j * P:(j + 1) * P], hot[:, u, j, :], ident[:])
                mm.then_inc(turned1[u], 1)

            def spread_B(m, u):
                pe.wait_ge(hotT_made1[u], (m + 1) * 2)
                pe.wait_ge(B_in1[u], (m + 1) * 16)
                v, c = two_back(u, m)
                pe.wait_ge(added1[v], c)
                for j in range(TILES):
                    mm = pe.matmul(z_ps[u % 2][:, j * D:(j + 1) * D], hotT[:, u % 2, j, :], B_win[:, u, :],
                                   start=True, stop=True)
                mm.then_inc(spread1[u], 1)

            for w in range(2):
                pe.wait_ge(AB_copied[w], BATCHES // 2)
            with pe.Fori(0, n_pass) as k:
                with pe.Fori(0, TURNS) as t:
                    m = pe.snap(k * TURNS + t)
                    turn_hot(m, 0)
                    for u in range(RING):
                        if u + 1 < RING:
                            turn_hot(m, u + 1)
                        spread_B(m, u)
                        if u >= 1:
                            segment_sums(m, u - 1, D + 1, msg_made1, hot_made1, sum_kept1, seg_done1)
                    segment_sums(m, RING - 1, D + 1, msg_made1, hot_made1, sum_kept1, seg_done1)

            with pe.Fori(0, BATCHES // 2) as i:
                for w in range(2):
                    project(1, i, w, W2_65)

        @block.vector
        def _(dve):
            dve.memset(zeros[:], 0.0).then_inc(dve_setup, 1)
            dve.memset(ln_eps[:], LN_EPS)
            dve.memset(ones[:], 1.0)
            dve.wait_ge(weights_in, 16 * 9)
            dve.tensor_scalar(one_eps[:], eps_in[:], 1.0, None, ALU.add).then_inc(dve_setup, 1)
            dve.wait_ge(dst_in, 16)
            dve.tensor_reduce(low_p[:], dst_i[:], AX.X, ALU.min)
            dve.tensor_reduce(high_p[:], dst_i[:], AX.X, ALU.max).then_inc(dve_setup, 1)
            dve.wait_ge(pe_setup, 1)
            for h in range(2):
                dve.tensor_reduce(low_g[:, h:h + 1], sum_ps[h][0:HALF, 0:P], AX.X, ALU.min)
                ins = dve.tensor_reduce(high_g[:, h:h + 1], z_ps[h][0:HALF, 0:P], AX.X, ALU.max)
            ins.then_inc(dve_setup, 1)
            dve.wait_ge(ident_made, 3)
            dve.wait_ge(dve_setup, 4)
            for h in range(2):
                dve.tensor_scalar(diag[:, h, :], ident[0:HALF, 0:HALF], low_g[:, h:h + 1], None, ALU.mult)
                ins = dve.tensor_scalar(diag[:, 2 + h, :], ident[0:HALF, 0:HALF], high_g[:, h:h + 1], None,
                                        ALU.mult)
            ins.then_inc(dve_setup, 1)
            dve.tensor_copy(window[:], iota_i[:])
            dve.memset(msg[:, :, :, D:D + 1], 1.0)
            dve.memset(x1T[D:D + 1], 1.0)
            dve.wait_ge(pe_setup, 2)
            dve.tensor_copy(WT65[0:D, :], wide_ps[0][0:D, 0:D]).then_inc(dve_setup, 1)
            dve.wait_ge(pe_setup, 3)
            for h in range(2):
                ins = dve.tensor_copy(low_all[:, h * HALF:(h + 1) * HALF], sum_ps[h][:, 0:HALF])
            ins.then_inc(dve_setup, 1)
            dve.wait_ge(dve_setup, 7)
            for h in range(2):
                ins = dve.tensor_tensor(span[:, h * HALF:(h + 1) * HALF], z_ps[h][:, 0:HALF],
                                        low_all[:, h * HALF:(h + 1) * HALF], ALU.subtract)
            ins.then_inc(dve_setup, 1)
            dve.tensor_copy(low_i[:], low_all[:])
            dve.tensor_tensor(dst_rel[:], dst_i[:], low_all[:].unsqueeze(2).to_broadcast([P, GROUPS, TILES]),
                              ALU.subtract).then_inc(dve_setup, 1)
            dve.wait_ge(dve_setup, 8)
            dve.tensor_reduce(span_max[:], span[:], AX.X, ALU.max).then_inc(dve_setup, 1)
            dve.wait_ge(dve_setup, 10)
            dve.tensor_copy(span_i[:], span_max[:]).then_inc(windows_known, 1)
            dve.memset(sum0[D:D + 1, :], 1.0).then_inc(dve_setup, 1)

            def make_hot(t, m, u, seg_sem, made_sem):
                dve.wait_ge(seg_sem[u], m)
                dve.tensor_tensor(
                    hot[:, u],
                    dst_rel[:, bass.ds(t * RING + u, 1), :].rearrange("p g j -> p (g j)").unsqueeze(2)
                    .to_broadcast([P, TILES, WIN]),
                    window[:].unsqueeze(1).to_broadcast([P, TILES, WIN]), ALU.is_equal,
                ).then_inc(made_sem[u], 1)

            def keep_sums(k, t, m, u, rows, sums, seg_sem, kept_sem):
                start = window_start(dve, k, t, u)
                dve.wait_ge(seg_sem[u], m + 1)
                if u == 0:
                    dve.wait_ge(kept_sem[RING - 1], m)
                else:
                    dve.wait_ge(kept_sem[u - 1], m + 1)
                cols = sums[0:rows, bass.ds(start, WIN)]
                dve.tensor_tensor(cols, sum_ps[u % 2][0:rows, 0:WIN], cols, ALU.add).then_inc(kept_sem[u], 1)

            def move_window(count):
                dve.tensor_scalar(window[:], window[:], float(WIN), None, ALU.add).then_inc(window_moved, 1)
                dve.wait_ge(window_moved, count)
                carry_wait(dve)

            for w in range(2):
                dve.wait_ge(x_scaled[w], BATCHES // 2)
            dve.wait_ge(dve_setup, 11)
            dve.wait_ge(pads_done, 16 * (4 + BATCHES))
            n_pass = passes(dve)
            with dve.Fori(0, n_pass) as k:
                with dve.Fori(0, TURNS) as t:
                    m = dve.snap(k * TURNS + t)
                    make_hot(t, m, 0, seg_done, hot_made)
                    for u in range(RING):
                        dve.wait_ge(gathered[u], (m + 1) * (16 * TILES))
                        dve.wait_ge(attr_in[u], (m + 1) * 16)
                        dve.tensor_tensor(gat[:, u, :], gat[:, u, :], attr[:, u, :], ALU.add
                                          ).then_inc(added[u], 1)
                        if u + 1 < RING:
                            make_hot(t, m, u + 1, seg_done, hot_made)
                        if u >= 1:
                            keep_sums(k, t, m, u - 1, D, sum0, seg_done, sum_kept)
                    keep_sums(k, t, m, RING - 1, D, sum0, seg_done, sum_kept)
                move_window(k + 1)

            def residual_and_norm(ph, i, relu):
                for w in range(2):
                    dve.wait_ge(proj_done[ph][w], i + 1)
                    dve.wait_ge(res_in[ph][w], (i + 1) * 16)
                    dve.wait_ge(norm_made[ph][w], i)
                    res = x_b[:, w, :].rearrange("p (c d) -> p c d", d=D)
                    proj = z_ps[w][:, 0:BLK * D].rearrange("p (c d) -> p c d", d=D)
                    if relu:
                        dve.scalar_tensor_tensor(out=y[:, w], in0=proj, scalar=0.0, in1=res,
                                                 op0=ALU.max, op1=ALU.add).then_inc(y_made[ph][w], 1)
                    else:
                        dve.tensor_tensor(y[:, w], proj, res, ALU.add).then_inc(y_made[ph][w], 1)
                for w in range(2):
                    dve.wait_ge(y_made[ph][w], i + 1)
                    for c in range(BLK):
                        ins = dve.bn_stats(stats[:, w, c, :], y[:, w, c, :])
                    ins.then_inc(stats_made[ph][w], 1)
                for w in range(2):
                    dve.wait_ge(stats_made[ph][w], i + 1)
                    carry_wait(dve)
                    for c in range(BLK):
                        ins = dve.bn_aggr(mean_var[:, w, c, :], stats[:, w, c, :])
                    ins.then_inc(var_made[ph][w], 1)
                for w in range(2):
                    dve.wait_ge(std_made[ph][w], i + 1)
                    dve.reciprocal(rstd[:, w, :], std[:, w, :]).then_inc(rstd_made[ph][w], 1)
                for w in range(2):
                    dve.wait_ge(rstd_made[ph][w], i + 1)
                    dve.wait_ge(norm_out[ph][w], i * 16)
                    if ph == 0:
                        dve.wait_ge(x1_turned[w], i)
                    for c in range(BLK):
                        ins = dve.tensor_scalar(x1_b[:, w, c, :], y[:, w, c, :], mean_var[:, w, c, 0:1],
                                                rstd[:, w, c:c + 1], ALU.subtract, ALU.mult)
                    ins.then_inc(norm_made[ph][w], 1)

            with dve.Fori(0, BATCHES // 2) as i:
                residual_and_norm(0, i, True)

            dve.tensor_copy(window[:], iota_i[:]).then_inc(window_moved, 1)
            dve.wait_ge(window_moved, n_pass + 1)
            carry_wait(dve)

            def edge_terms(m, u):
                w = u % 2
                dve.wait_ge(ew_in1[u], (m + 1) * 16)
                v, c = two_back(u, m)
                dve.wait_ge(part_added1[v], c)
                dve.tensor_tensor(edge_term[:, w], ew_in[:, u, :].unsqueeze(2).to_broadcast([P, TILES, D]),
                                  w_edge[:].unsqueeze(1).to_broadcast([P, TILES, D]), ALU.mult
                                  ).then_inc(edge_term1[u], 1)

            def add_terms(m, u):
                w = u % 2
                rows = gat[:, u, :].rearrange("p (j d) -> p j d", d=D)
                dve.wait_ge(gathered1[u], (m + 1) * (16 * TILES))
                dve.wait_ge(edge_term1[u], m + 1)
                dve.tensor_tensor(rows, rows, edge_term[:, w], ALU.add).then_inc(part_added1[u], 1)
                dve.wait_ge(part_added1[u], m + 1)
                dve.wait_ge(spread1[u], m + 1)
                dve.tensor_tensor(gat[:, u, :], z_ps[w][:], gat[:, u, :], ALU.add).then_inc(added1[u], 1)

            with dve.Fori(0, n_pass) as k:
                with dve.Fori(0, TURNS) as t:
                    m = dve.snap(k * TURNS + t)
                    make_hot(t, m, 0, seg_done1, hot_made1)
                    edge_terms(m, 0)
                    for u in range(RING):
                        if u + 1 < RING:
                            make_hot(t, m, u + 1, seg_done1, hot_made1)
                            edge_terms(m, u + 1)
                        add_terms(m, u)
                        if u >= 1:
                            keep_sums(k, t, m, u - 1, D + 1, sum1, seg_done1, sum_kept1)
                    keep_sums(k, t, m, RING - 1, D + 1, sum1, seg_done1, sum_kept1)
                move_window(n_pass + 2 + k)

            with dve.Fori(0, BATCHES // 2) as i:
                residual_and_norm(1, i, False)


def kernel(x, src, dst, edge_attr_64, edge_weight1, L0_gnn_W, L0_gnn_b, L0_gnn_eps, L1_gnn_W1, L1_gnn_b1,
           L1_gnn_W2, L1_gnn_b2):
    import numpy as np
    import concourse.bacc as bacc
    from concourse.bass_utils import run_bass_kernel_spmd

    def padded(a, rows, value=0):
        a = np.ascontiguousarray(a)
        return np.concatenate([a, np.full((rows - a.shape[0],) + a.shape[1:], value, a.dtype)])

    def row(a):
        return np.ascontiguousarray(a).reshape(1, -1)

    arrays = {
        "x": padded(x, N_PAD),
        "src": padded(src, E_PAD),
        "dst": padded(dst, E_PAD, N),
        "ea": padded(edge_attr_64, E_PAD),
        "ew": padded(edge_weight1, E_PAD),
        "W": np.ascontiguousarray(L0_gnn_W),
        "b": row(L0_gnn_b),
        "eps": row(L0_gnn_eps),
        "W1": np.ascontiguousarray(L1_gnn_W1),
        "b1": row(L1_gnn_b1),
        "W2": np.ascontiguousarray(L1_gnn_W2),
        "b2": row(L1_gnn_b2),
    }
    arrays = {f"in_{name}": a for name, a in arrays.items()}
    nc = bacc.Bacc("TRN2", target_bir_lowering=False, num_devices=1)
    args = [nc.dram_tensor(name, a.shape, mybir.dt.from_np(a.dtype), kind="ExternalInput").ap()
            for name, a in arrays.items()]
    out = nc.dram_tensor("out_nodes", (N_PAD, D), F32, kind="ExternalOutput").ap()
    build(nc, *args, out)
    results = run_bass_kernel_spmd(nc, [arrays], core_ids=[0]).results
    return results[0]["out_nodes"][:N]
```

```python
from contextlib import ExitStack

import concourse.bass as bass
from concourse import mybir

F32 = mybir.dt.float32
I32 = mybir.dt.int32
ALU = mybir.AluOpType
ACT = mybir.ActivationFunctionType
AX = mybir.AxisListType

P = 128
D = 64
N = 12500
E = 200000
TILES = 8
GROUP = P * TILES
RING = 7
TURNS = -(-E // (GROUP * RING))
GROUPS = TURNS * RING
E_PAD = GROUPS * GROUP
LAST_EDGES = E - (GROUPS - 1) * GROUP
LAST_TILES = -(-LAST_EDGES // P)
WIN = 96
BLK = 7
BANK_ROWS = 4
BATCH = P * BLK
BATCHES = -(-N // BATCH)
N_PAD = BATCHES * BATCH
COLS = N_PAD + WIN
HALF = GROUPS // 2
LN_EPS = 1e-5
ZERO_COLS = 790
STEPS = 5
assert HALF <= P and N < N_PAD and COLS % ZERO_COLS == 0 and TURNS < 2 ** STEPS and BATCHES <= WIN


def last_user(u, m):
    return (u - 2, m + 1) if u >= 2 else (RING - 1 - (RING - 1 - u) % 2, m)


def build(nc, x, src, dst, ea, ew, W, b, eps, W1, b1, W2, b2, out):
    ctx = ExitStack()
    with ctx:
        def sb(name, shape, dt=F32):
            return ctx.enter_context(nc.sbuf_tensor(name, shape, dt))

        def ps(name, cols):
            return ctx.enter_context(nc.psum_tensor(name, [P, cols], F32))

        def sem(name):
            return ctx.enter_context(nc.semaphore(name))

        def ring_sem(name):
            return [sem(f"{name}{u}") for u in range(RING)]

        A_dram = nc.dram_tensor("A_dram", (N_PAD, D), F32).ap()
        B_dram = nc.dram_tensor("B_dram", (COLS, D), F32).ap()
        x1_dram = nc.dram_tensor("x1_dram", (N_PAD, D), F32).ap()

        ident = sb("ident", [P, P])
        iota_i = sb("iota_i", [P, WIN], I32)
        window = sb("window", [P, WIN])
        ones = sb("ones", [P, P])
        zeros = sb("zeros", [P, ZERO_COLS])
        W_in = sb("W_in", [D, D])
        WT65 = sb("WT65", [D + 1, D])
        W1AB = sb("W1AB", [D + 1, 2 * D])
        W2_65 = sb("W2_65", [D + 1, D])
        w_edge = sb("w_edge", [P, D])
        eps_in = sb("eps_in", [D, 1])
        one_eps = sb("one_eps", [D, 1])
        ln_eps = sb("ln_eps", [P, 1])

        dst_i = sb("dst_i", [P, GROUPS, TILES], I32)
        dst_rel = sb("dst_rel", [P, GROUPS, TILES])
        low_g = sb("low_g", [HALF, 2])
        high_g = sb("high_g", [HALF, 2])
        diag = sb("diag", [HALF, 4, HALF])
        low_all = sb("low_all", [P, GROUPS])
        span = sb("span", [P, GROUPS])
        span_max = sb("span_max", [P, 1])
        low_i = sb("low_i", [P, GROUPS], I32)
        span_i = sb("span_i", [P, 1], I32)
        low_behind = sb("low_behind", [P, 2, TURNS + 2 ** (STEPS - 1)])
        batch_end = sb("batch_end", [P, BATCHES])
        is_final = sb("is_final", [P, TURNS, BATCHES])
        n_final = sb("n_final", [P, TURNS])
        final_i = sb("final_i", [P, TURNS + 1], I32)

        sum0 = sb("sum0", [D, COLS])
        sum1 = sb("sum1", [D + 1, COLS])

        idx = sb("idx", [P, RING, TILES], I32)
        attr = sb("attr", [P, RING, TILES * D])
        gat = sb("gat", [P, RING, TILES * D])
        msg = sb("msg", [P, RING, TILES, D + 1])
        hot = sb("hot", [P, RING, TILES, WIN])
        ew_t = sb("ew_t", [P, RING, TILES])
        B_win = sb("B_win", [WIN, RING, D])

        hotT = attr[0:WIN, 0:4, :].rearrange("p (w h) (j q) -> p w (h j) q", w=2, q=P)
        edge_term = attr[:, 4:6, :].rearrange("p w (j d) -> p w j d", d=D)

        dst_rows = hot.ap().rearrange("p u j q -> p (u j q)")[0:HALF, 0:2 * GROUP].rearrange(
            "p (h e) -> p h e", h=2).bitcast(I32)

        x_b = sb("x_b", [P, BLK, D])
        hT = sb("hT", [D + 1, BLK, P])
        y = sb("y", [P, BLK, D])
        stats = sb("stats", [P, BLK, 6])
        mean_var = sb("mean_var", [P, BLK, 2])
        std = sb("std", [P, BLK])
        rstd = sb("rstd", [P, BLK])
        x1_b = sb("x1_b", [P, BLK, D])
        x1T = sb("x1T", [D + 1, BLK, P])
        AB_b = sb("AB_b", [P, 2, BLK, D])

        sum_ps = [ps(f"sum_ps{w}", 512) for w in range(2)]
        z_ps = [ps(f"z_ps{w}", 512) for w in range(2)]
        wide_ps = [ps(f"wide_ps{w}", 1024) for w in range(2)]

        waits_carried = sem("waits_carried")
        weights_in = sem("weights_in")
        rows_in = sem("rows_in")
        dst_in = sem("dst_in")
        ident_made = sem("ident_made")
        zeros_made = sem("zeros_made")
        dve_setup = sem("dve_setup")
        pe_setup = sem("pe_setup")
        sums_cleared = sem("sums_cleared")
        windows_known = sem("windows_known")
        window_moved = sem("window_moved")
        idx_in = ring_sem("idx_in")
        gathered = ring_sem("gathered")
        hot_made = ring_sem("hot_made")
        added = ring_sem("added")
        msg_made = ring_sem("msg_made")
        seg_done = ring_sem("seg_done")
        sum_kept = ring_sem("sum_kept")
        attr_in = ring_sem("attr_in")
        ew_in = ring_sem("ew_in")
        B_in = ring_sem("B_in")
        hot_turned = ring_sem("hot_turned")
        hotT_made = ring_sem("hotT_made")
        B_spread = ring_sem("B_spread")
        term_made = ring_sem("term_made")
        term_added = ring_sem("term_added")
        res_in = sem("res_in")
        hT_made = sem("hT_made")
        proj_done = sem("proj_done")
        y_made = sem("y_made")
        stats_made = sem("stats_made")
        var_made = sem("var_made")
        std_made = sem("std_made")
        rstd_made = sem("rstd_made")
        norm_made = sem("norm_made")
        stored = sem("stored")
        x_turned = sem("x_turned")
        x1_turned = sem("x1_turned")
        x1T_made = sem("x1T_made")
        AB_done = sem("AB_done")
        AB_low_copied = sem("AB_low_copied")
        AB_high_copied = sem("AB_high_copied")

        dst_v = dst.rearrange("(g p j) -> p g j", p=P, j=TILES)

        def edges(t, u):
            return (t * RING + u) * GROUP

        def src_v(t, u):
            return src[bass.ds(edges(t, u), GROUP)].rearrange("(p j) -> p j", p=P)

        def ea_v(t, u):
            return ea[bass.ds(edges(t, u), GROUP), :].rearrange("(p j) d -> p (j d)", p=P)

        def ew_v(t, u):
            return ew[bass.ds(edges(t, u), GROUP), :].rearrange("(p j) o -> p (j o)", p=P)

        def batch_v(dram, s):
            return dram[bass.ds(s * BATCH, BATCH), :].rearrange("(p c) d -> p c d", p=P)

        def cols_v(sums, s):
            return sums[:, bass.ds(s * BATCH, BATCH)].rearrange("k (p c) -> k c p", p=P)

        def AB_part(first, end):
            return (wide_ps[0][:, first * 2 * D:end * 2 * D].rearrange("p (r a d) -> p r a d", a=2, d=D),
                    AB_b[:, :, first:end, :].rearrange("p a r d -> p r a d"))

        def passes(eng):
            eng.wait_ge(windows_known, 1)
            return eng.snap(eng.value_load(span_i[0:1, 0:1], min_val=0, max_val=N_PAD - 1) // WIN + 1,
                            min_val=1, max_val=COLS // WIN)

        def window_start(eng, k, t, u):
            low = eng.value_load(low_i[0:1, bass.ds(t * RING + u, 1)], min_val=0, max_val=N_PAD - 1)
            start = start_regs[eng.engine]
            eng.reg_mov(start, low + k * WIN)
            eng.reg_alu(start, start, N_PAD, op=ALU.min)
            return eng.snap(start, min_val=0, max_val=N_PAD)

        ALL_STORED = 16 * (1 + 3 * BATCHES)

        start_regs = {eng.engine: eng.alloc_register("window_start") for eng in (nc.sync, nc.vector)}

        def carry_wait(eng):
            eng.sem_inc(waits_carried, 1)

        def first_credit(eng, *rings):
            for ring in rings:
                for u in range(RING):
                    eng.sem_inc(ring[u], 1)

        def turn_no(eng, k, t):
            return eng.snap(k * TURNS + t + 1)

        def each_turn(eng, layer, n_pass, body, batch, after_pass=None):
            with eng.Fori(0, n_pass) as k:
                with eng.Fori(0, TURNS) as t:
                    own = turn_no(eng, k, t)
                    m = turn_no(eng, k + n_pass, t) if layer else own
                    body(k, t, m, own)
                    last = k + 1 >= n_pass
                    before = eng.value_load(final_i[0:1, bass.ds(t, 1)], min_val=0, max_val=BATCHES)
                    after = eng.value_load(final_i[0:1, bass.ds(t + 1, 1)], min_val=0, max_val=BATCHES)
                    first = eng.snap(before * last, min_val=0, max_val=BATCHES)
                    end = eng.snap(after * last, min_val=0, max_val=BATCHES)
                    with eng.If(end > first):
                        with eng.Fori(first, end) as s:
                            batch(s, s + layer * BATCHES, m)
                        carry_wait(eng)
                if after_pass:
                    after_pass(k)

        block = ctx.enter_context(nc.Block())

        @block.sync
        def _(sp):
            def load_groups0(k):
                with sp.Fori(0, TURNS) as t:
                    m = turn_no(sp, k, t)
                    for u in range(RING):
                        sp.wait_ge(added[u], m)
                        sp.dma_start(idx[:, u, :], src_v(t, u)).then_inc(idx_in[u], 16)
                        sp.dma_start(attr[:, u, :], ea_v(t, u)).then_inc(attr_in[u], 16)

            load_groups0(0)
            n_pass = passes(sp)
            with sp.If(n_pass > 1):
                with sp.Fori(1, n_pass) as k:
                    load_groups0(k)
                carry_wait(sp)

            for u in range(RING):
                sp.wait_ge(added[u], n_pass * TURNS + 1)
            carry_wait(sp)
            with sp.Fori(0, n_pass) as k:
                with sp.Fori(0, TURNS) as t:
                    own = turn_no(sp, k, t)
                    for u in range(RING):
                        sp.wait_ge(term_added[u], own)
                        sp.dma_start(idx[:, u, :], src_v(t, u)).then_inc(idx_in[u], 16)
                        sp.wait_ge(term_made[u], own)
                        sp.dma_start(ew_t[:, u, :], ew_v(t, u)).then_inc(ew_in[u], 16)
                        start = window_start(sp, k, t, u)
                        sp.wait_ge(stored, ALL_STORED)
                        sp.wait_ge(B_spread[u], own)
                        sp.dma_start(B_win[:, u, :], B_dram[bass.ds(start, WIN), :]).then_inc(B_in[u], 16)

        @block.gpsimd
        def _(pool):
            pool.memset(ident[:], 0.0).then_inc(ident_made, 1)
            pool.iota(iota_i[:], pattern=[[1, WIN]], base=0, channel_multiplier=0).then_inc(ident_made, 1)
            pool.wait_ge(ident_made, 2)
            pool.affine_select(out=ident[:], in_=ident[:], compare_op=ALU.not_equal, fill=1.0, base=0,
                               pattern=[[-1, P]], channel_multiplier=1).then_inc(ident_made, 1)

            def gather_group(table, m, u, tiles):
                pool.wait_ge(idx_in[u], m * 16)
                pool.wait_ge(msg_made[u], m)
                carry_wait(pool)
                for j in range(tiles):
                    pool.indirect_dma_start(
                        out=gat[:, u, j * D:(j + 1) * D], out_offset=None, in_=table[:, :],
                        in_offset=bass.IndirectOffsetOnAxis(ap=idx[:, u, j:j + 1], axis=0),
                    ).then_inc(gathered[u], 16 if j + 1 < tiles else 16 * (TILES + 1 - tiles))

            def gather_pass(table, k):
                with pool.Fori(0, TURNS - 1) as t:
                    for u in range(RING):
                        gather_group(table, turn_no(pool, k, t), u, TILES)
                m = turn_no(pool, k, TURNS - 1)
                for u in range(RING - 1):
                    gather_group(table, m, u, TILES)
                gather_group(table, m, RING - 1, LAST_TILES)

            gather_pass(x, 0)
            n_pass = passes(pool)
            with pool.If(n_pass > 1):
                with pool.Fori(1, n_pass) as k:
                    gather_pass(x, k)
                carry_wait(pool)
            pool.wait_ge(stored, ALL_STORED)
            with pool.Fori(0, n_pass) as k:
                gather_pass(A_dram, k + n_pass)

        @block.scalar
        def _(act):
            first_credit(act, msg_made, hotT_made)
            act.dma_start(dst_rows, dst.rearrange("(h p e) -> p h e", h=2, p=HALF)).then_inc(rows_in, 16)
            act.wait_ge(zeros_made, 1)
            act.dma_start(sum0.ap().rearrange("p (r c) -> p r c", c=ZERO_COLS),
                          zeros[0:D, :].unsqueeze(1).to_broadcast([D, COLS // ZERO_COLS, ZERO_COLS])
                          ).then_inc(sums_cleared, 16)
            act.dma_start(dst_i[:], dst_v).then_inc(dst_in, 16)
            act.dma_start(eps_in[:], eps.to_broadcast([D, 1])).then_inc(weights_in, 16)
            act.dma_start(W_in[:], W).then_inc(weights_in, 16)
            act.dma_start(WT65[D:D + 1, :], b).then_inc(weights_in, 16)
            act.dma_start(W1AB[0:D, 0:D], W1[0:D, :]).then_inc(weights_in, 16)
            act.dma_start(W1AB[0:D, D:2 * D], W1[D:2 * D, :]).then_inc(weights_in, 16)
            act.dma_start(W1AB[D:D + 1, 0:D], b1).then_inc(weights_in, 16)
            act.dma_start(W1AB[D:D + 1, D:2 * D], zeros[0:1, 0:D]).then_inc(weights_in, 16)
            act.dma_start(W2_65[0:D, :], W2).then_inc(weights_in, 16)
            act.dma_start(W2_65[D:D + 1, :], b2).then_inc(weights_in, 16)
            act.dma_start(w_edge[:], W1[2 * D:2 * D + 1, :].to_broadcast([P, D])).then_inc(weights_in, 16)
            act.dma_start(B_dram[N_PAD:COLS, :], zeros[0:WIN, 0:D]).then_inc(stored, 16)
            act.dma_start(sum1.ap().rearrange("p (r c) -> p r c", c=ZERO_COLS),
                          zeros[0:D + 1, :].unsqueeze(1).to_broadcast([D + 1, COLS // ZERO_COLS, ZERO_COLS])
                          ).then_inc(sums_cleared, 16)

            def relu(m, u):
                act.wait_ge(added[u], m + 1)
                act.wait_ge(seg_done[u], m)
                act.activation(msg[:, u, :, 0:D], gat[:, u, :].rearrange("p (j d) -> p j d", d=D),
                               ACT.Relu).then_inc(msg_made[u], 1)

            def root(c):
                act.wait_ge(var_made, c + 1)
                act.activation(std[:], mean_var[:, :, 1], ACT.Sqrt, bias=ln_eps[:, 0:1]).then_inc(std_made, 1)

            def turn0(k, t, m, own):
                for u in range(RING):
                    relu(m, u)

            def batch0(s, c, m):
                act.dma_start(x_b[:], batch_v(x, s)).then_inc(res_in, 16)
                root(c)
                act.wait_ge(norm_made, c + 1)
                act.dma_start(batch_v(x1_dram, s), x1_b[:]).then_inc(stored, 16)
                act.wait_ge(x1_turned, s + 1)
                act.activation(x1T[0:D], wide_ps[1][0:D, 0:BATCH].rearrange("k (c p) -> k c p", p=P),
                               ACT.Copy).then_inc(x1T_made, 1)
                act.wait_ge(AB_done, s + 1)
                AB_ps, AB_rows = AB_part(0, BANK_ROWS)
                act.activation(AB_rows, AB_ps, ACT.Copy).then_inc(AB_low_copied, 1)
                act.wait_ge(AB_low_copied, s + 1)
                act.wait_ge(AB_high_copied, s + 1)
                act.dma_start(batch_v(A_dram, s), AB_b[:, 0]).then_inc(stored, 16)
                act.dma_start(batch_v(B_dram, s), AB_b[:, 1]).then_inc(stored, 16)

            n_pass = passes(act)
            each_turn(act, 0, n_pass, turn0, batch0)

            def copy_turned(own, u):
                act.wait_ge(hot_turned[u], own + 1)
                v, c = last_user(u, own)
                act.wait_ge(B_spread[v], c)
                act.activation(hotT[:, u % 2], wide_ps[u % 2][0:WIN].rearrange("p (j q) -> p j q", q=P),
                               ACT.Copy).then_inc(hotT_made[u], 1)

            def turn1(k, t, m, own):
                copy_turned(own, 0)
                for u in range(RING):
                    if u + 1 < RING:
                        copy_turned(own, u + 1)
                    relu(m, u)

            def batch1(s, c, m):
                act.dma_start(x_b[:], batch_v(x1_dram, s)).then_inc(res_in, 16)
                root(c)
                act.wait_ge(norm_made, c + 1)
                act.dma_start(batch_v(out, s), x1_b[:]).then_inc(stored, 16)

            each_turn(act, 1, n_pass, turn1, batch1)
            act.wait_ge(stored, ALL_STORED + 16 * BATCHES)

        @block.tensor
        def _(pe):
            first_credit(pe, seg_done, hot_turned, B_spread)
            pe.wait_ge(ident_made, 3)
            pe.wait_ge(dve_setup, 3)
            for h in range(2):
                pe.matmul(sum_ps[h][:, 0:HALF], ones[0:HALF, :], diag[:, h, :], start=True, stop=True)
                mm = pe.matmul(z_ps[h][:, 0:HALF], ones[0:HALF, :], diag[:, 2 + h, :], start=True, stop=True)
            mm.then_inc(pe_setup, 1)
            pe.wait_ge(weights_in, 16 * 10)
            pe.transpose(wide_ps[0][0:D, 0:D], W_in[:], ident[0:D, 0:D]).then_inc(pe_setup, 1)

            def segment_sums(m, u, rows):
                pe.wait_ge(msg_made[u], m + 1)
                pe.wait_ge(hot_made[u], m + 1)
                v, c = last_user(u, m)
                pe.wait_ge(sum_kept[v], c)
                for j in range(TILES):
                    mm = pe.matmul(sum_ps[u % 2][0:rows, 0:WIN], msg[:, u, j, 0:rows], hot[:, u, j, :],
                                   start=(j == 0), stop=(j == TILES - 1))
                mm.then_inc(seg_done[u], 1)

            def project(c, weights):
                pe.wait_ge(hT_made, c + 1)
                for r in range(BLK):
                    mm = pe.matmul(z_ps[0][:, r * D:(r + 1) * D], hT[:, r, :], weights[:], start=True, stop=True)
                mm.then_inc(proj_done, 1)

            def turn0(k, t, m, own):
                for u in range(RING):
                    segment_sums(m, u, D)

            def batch0(s, c, m):
                pe.wait_ge(res_in, s * 16 + 16)
                carry_wait(pe)
                for r in range(BLK):
                    mm = pe.transpose(wide_ps[0][0:D, r * P:(r + 1) * P], x_b[:, r, :], ident[:])
                mm.then_inc(x_turned, 1)
                project(c, WT65)
                pe.wait_ge(norm_made, c + 1)
                carry_wait(pe)
                for r in range(BLK):
                    mm = pe.transpose(wide_ps[1][0:D, r * P:(r + 1) * P], x1_b[:, r, :], ident[:])
                mm.then_inc(x1_turned, 1)
                pe.wait_ge(x1T_made, s + 1)
                for r in range(BLK):
                    mm = pe.matmul(wide_ps[0][:, r * P:(r + 1) * P], x1T[:, r, :], W1AB[:], start=True, stop=True)
                mm.then_inc(AB_done, 1)
                pe.wait_ge(AB_low_copied, s + 1)
                pe.wait_ge(AB_high_copied, s + 1)
                carry_wait(pe)

            pe.wait_ge(windows_known, 1)
            n_pass = passes(pe)
            each_turn(pe, 0, n_pass, turn0, batch0)

            def turn_hot(m, own, u):
                pe.wait_ge(hot_made[u], m + 1)
                v, c = last_user(u, own)
                pe.wait_ge(hotT_made[v], c)
                for j in range(TILES):
                    mm = pe.transpose(wide_ps[u % 2][0:WIN, j * P:(j + 1) * P], hot[:, u, j, :], ident[:])
                mm.then_inc(hot_turned[u], 1)

            def spread_B(m, own, u):
                pe.wait_ge(hotT_made[u], own + 1)
                pe.wait_ge(B_in[u], own * 16)
                v, c = last_user(u, m)
                pe.wait_ge(added[v], c)
                for j in range(TILES):
                    mm = pe.matmul(z_ps[u % 2][:, j * D:(j + 1) * D], hotT[:, u % 2, j, :], B_win[:, u, :],
                                   start=True, stop=True)
                mm.then_inc(B_spread[u], 1)

            def turn1(k, t, m, own):
                turn_hot(m, own, 0)
                for u in range(RING):
                    if u + 1 < RING:
                        turn_hot(m, own, u + 1)
                    spread_B(m, own, u)
                    if u >= 1:
                        segment_sums(m, u - 1, D + 1)
                segment_sums(m, RING - 1, D + 1)

            def batch1(s, c, m):
                project(c, W2_65)
                pe.wait_ge(y_made, c + 1)
                carry_wait(pe)

            each_turn(pe, 1, n_pass, turn1, batch1)

        @block.vector
        def _(dve):
            first_credit(dve, hot_made, added, sum_kept, term_made, term_added)
            dve.memset(zeros[:], 0.0).then_inc(zeros_made, 1)
            dve.memset(ln_eps[:], LN_EPS)
            dve.memset(ones[:], 1.0).then_inc(dve_setup, 1)
            dve.wait_ge(rows_in, 16)
            dve.tensor_reduce(low_g[:], dst_rows, AX.X, ALU.min)
            dve.tensor_reduce(high_g[:], dst_rows, AX.X, ALU.max).then_inc(dve_setup, 1)
            dve.wait_ge(ident_made, 3)
            dve.wait_ge(dve_setup, 2)
            for h in range(2):
                dve.tensor_scalar(diag[:, h, :], ident[0:HALF, 0:HALF], low_g[:, h:h + 1], None, ALU.mult)
                ins = dve.tensor_scalar(diag[:, 2 + h, :], ident[0:HALF, 0:HALF], high_g[:, h:h + 1], None,
                                        ALU.mult)
            ins.then_inc(dve_setup, 1)
            dve.tensor_copy(window[:], iota_i[:])
            dve.tensor_scalar(batch_end[:], iota_i[:, 0:BATCHES], 1.0, float(BATCH), ALU.add, ALU.mult)
            dve.memset(low_behind[:], float(N_PAD))
            dve.memset(final_i[:], 0)
            dve.memset(msg[:, :, :, D:D + 1], 1.0)
            dve.memset(hT[D:D + 1], 1.0)
            dve.memset(x1T[D:D + 1], 1.0)
            dve.wait_ge(pe_setup, 1)
            for h in range(2):
                ins = dve.tensor_copy(low_all[:, h * HALF:(h + 1) * HALF], sum_ps[h][:, 0:HALF])
            ins.then_inc(dve_setup, 1)
            dve.wait_ge(dve_setup, 4)
            for h in range(2):
                ins = dve.tensor_tensor(span[:, h * HALF:(h + 1) * HALF], z_ps[h][:, 0:HALF],
                                        low_all[:, h * HALF:(h + 1) * HALF], ALU.subtract)
            dve.tensor_copy(low_i[:], low_all[:])
            dve.tensor_reduce(low_behind[:, 0, 0:TURNS], low_all[:].rearrange("p (t u) -> p t u", u=RING),
                              AX.X, ALU.min).then_inc(dve_setup, 1)
            dve.wait_ge(dve_setup, 5)
            dve.tensor_reduce(span_max[:], span[:], AX.X, ALU.max)
            for n in range(STEPS):
                now, then = n % 2, 1 - n % 2
                dve.tensor_tensor(low_behind[:, then, 0:TURNS], low_behind[:, now, 0:TURNS],
                                  low_behind[:, now, 2 ** n:2 ** n + TURNS], ALU.min).then_inc(dve_setup, 1)
                dve.wait_ge(dve_setup, 6 + n)
            dve.tensor_tensor(is_final[:],
                              low_behind[:, STEPS % 2, 1:TURNS + 1].unsqueeze(2).to_broadcast([P, TURNS, BATCHES]),
                              batch_end[:].unsqueeze(1).to_broadcast([P, TURNS, BATCHES]), ALU.is_ge
                              ).then_inc(dve_setup, 1)
            dve.tensor_copy(span_i[:], span_max[:])
            dve.wait_ge(dve_setup, 6 + STEPS)
            dve.tensor_reduce(n_final[:], is_final[:], AX.X, ALU.add).then_inc(dve_setup, 1)
            dve.wait_ge(weights_in, 16 * 10)
            dve.tensor_scalar(one_eps[:], eps_in[:], 1.0, None, ALU.add)
            dve.wait_ge(pe_setup, 2)
            dve.tensor_copy(WT65[0:D, :], wide_ps[0][0:D, 0:D])
            dve.wait_ge(dst_in, 16)
            dve.tensor_tensor(dst_rel[:], dst_i[:], low_all[:].unsqueeze(2).to_broadcast([P, GROUPS, TILES]),
                              ALU.subtract)
            dve.wait_ge(dve_setup, 7 + STEPS)
            dve.tensor_copy(final_i[:, 1:TURNS + 1], n_final[:]).then_inc(windows_known, 1)

            def make_hot(t, m, u):
                dve.wait_ge(seg_done[u], m)
                dve.tensor_tensor(
                    hot[:, u],
                    dst_rel[:, bass.ds(t * RING + u, 1), :].rearrange("p g j -> p (g j)").unsqueeze(2)
                    .to_broadcast([P, TILES, WIN]),
                    window[:].unsqueeze(1).to_broadcast([P, TILES, WIN]), ALU.is_equal,
                ).then_inc(hot_made[u], 1)

            def keep_sums(k, t, m, u, rows, sums):
                start = window_start(dve, k, t, u)
                dve.wait_ge(seg_done[u], m + 1)
                if u == 0:
                    dve.wait_ge(sum_kept[RING - 1], m)
                else:
                    dve.wait_ge(sum_kept[u - 1], m + 1)
                cols = sums[0:rows, bass.ds(start, WIN)]
                dve.tensor_tensor(cols, sum_ps[u % 2][0:rows, 0:WIN], cols, ALU.add).then_inc(sum_kept[u], 1)

            def residual_and_norm(layer, c, stored_before):
                dve.wait_ge(proj_done, c + 1)
                dve.wait_ge(res_in, c * 16 + 16)
                proj = z_ps[0][:, 0:BLK * D].rearrange("p (c d) -> p c d", d=D)
                if layer == 0:
                    dve.scalar_tensor_tensor(out=y[:], in0=proj, scalar=0.0, in1=x_b[:],
                                             op0=ALU.max, op1=ALU.add).then_inc(y_made, 1)
                else:
                    dve.tensor_tensor(y[:], proj, x_b[:], ALU.add).then_inc(y_made, 1)
                dve.wait_ge(y_made, c + 1)
                for r in range(BLK):
                    ins = dve.bn_stats(stats[:, r, :], y[:, r, :])
                ins.then_inc(stats_made, 1)
                dve.wait_ge(stats_made, c + 1)
                carry_wait(dve)
                for r in range(BLK):
                    ins = dve.bn_aggr(mean_var[:, r, :], stats[:, r, :])
                ins.then_inc(var_made, 1)
                dve.wait_ge(std_made, c + 1)
                dve.reciprocal(rstd[:], std[:]).then_inc(rstd_made, 1)
                dve.wait_ge(rstd_made, c + 1)
                dve.wait_ge(stored, stored_before)
                for r in range(BLK):
                    ins = dve.tensor_scalar(x1_b[:, r, :], y[:, r, :], mean_var[:, r, 0:1],
                                            rstd[:, r:r + 1], ALU.subtract, ALU.mult)
                ins.then_inc(norm_made, 1)

            def turn0(k, t, m, own):
                make_hot(t, m, 0)
                for u in range(RING):
                    dve.wait_ge(gathered[u], m * (16 * TILES))
                    dve.wait_ge(attr_in[u], m * 16)
                    dve.tensor_tensor(gat[:, u, :], gat[:, u, :], attr[:, u, :], ALU.add).then_inc(added[u], 1)
                    if u + 1 < RING:
                        make_hot(t, m, u + 1)
                    if u >= 1:
                        keep_sums(k, t, m, u - 1, D, sum0)
                keep_sums(k, t, m, RING - 1, D, sum0)

            def batch0(s, c, m):
                dve.wait_ge(x_turned, s + 1)
                dve.wait_ge(sum_kept[RING - 1], m + 1)
                dve.scalar_tensor_tensor(out=hT[0:D], in0=wide_ps[0][0:D, 0:BATCH].rearrange("k (c p) -> k c p", p=P),
                                         scalar=one_eps[:, 0:1], in1=cols_v(sum0, s),
                                         op0=ALU.mult, op1=ALU.add).then_inc(hT_made, 1)
                residual_and_norm(0, c, s * 48 + 16)
                dve.wait_ge(AB_done, s + 1)
                AB_ps, AB_rows = AB_part(BANK_ROWS, BLK)
                dve.tensor_copy(AB_rows, AB_ps).then_inc(AB_high_copied, 1)

            def move_window(before, k):
                dve.tensor_scalar(window[:], window[:], float(WIN), None, ALU.add).then_inc(window_moved, 1)
                dve.wait_ge(window_moved, before + k + 1)
                carry_wait(dve)

            n_pass = passes(dve)
            dve.wait_ge(sums_cleared, 32)
            each_turn(dve, 0, n_pass, turn0, batch0, lambda k: move_window(0, k))

            dve.tensor_copy(window[:], iota_i[:]).then_inc(window_moved, 1)
            dve.wait_ge(window_moved, n_pass + 1)
            carry_wait(dve)

            def edge_terms(own, u):
                dve.wait_ge(ew_in[u], own * 16)
                v, c = last_user(u, own)
                dve.wait_ge(term_added[v], c)
                dve.tensor_tensor(edge_term[:, u % 2], ew_t[:, u, :].unsqueeze(2).to_broadcast([P, TILES, D]),
                                  w_edge[:].unsqueeze(1).to_broadcast([P, TILES, D]), ALU.mult
                                  ).then_inc(term_made[u], 1)

            def add_terms(m, own, u):
                rows = gat[:, u, :].rearrange("p (j d) -> p j d", d=D)
                dve.wait_ge(gathered[u], m * (16 * TILES))
                dve.wait_ge(term_made[u], own + 1)
                dve.tensor_tensor(rows, rows, edge_term[:, u % 2], ALU.add).then_inc(term_added[u], 1)
                dve.wait_ge(term_added[u], own + 1)
                dve.wait_ge(B_spread[u], own + 1)
                dve.tensor_tensor(gat[:, u, :], z_ps[u % 2][:], gat[:, u, :], ALU.add).then_inc(added[u], 1)

            def turn1(k, t, m, own):
                make_hot(t, m, 0)
                edge_terms(own, 0)
                for u in range(RING):
                    if u + 1 < RING:
                        make_hot(t, m, u + 1)
                        edge_terms(own, u + 1)
                    add_terms(m, own, u)
                    if u >= 1:
                        keep_sums(k, t, m, u - 1, D + 1, sum1)
                keep_sums(k, t, m, RING - 1, D + 1, sum1)

            def batch1(s, c, m):
                dve.wait_ge(sum_kept[RING - 1], m + 1)
                dve.wait_ge(proj_done, c)
                dve.tensor_copy(hT[:], cols_v(sum1, s)).then_inc(hT_made, 1)
                residual_and_norm(1, c, s * 16 + ALL_STORED)

            each_turn(dve, 1, n_pass, turn1, batch1, lambda k: move_window(n_pass + 1, k))


def kernel(x, src, dst, edge_attr_64, edge_weight1, L0_gnn_W, L0_gnn_b, L0_gnn_eps, L1_gnn_W1, L1_gnn_b1,
           L1_gnn_W2, L1_gnn_b2):
    import numpy as np
    import concourse.bacc as bacc
    from concourse.bass_utils import run_bass_kernel_spmd

    def padded(a, rows, value=0):
        a = np.ascontiguousarray(a)
        return np.concatenate([a, np.full((rows - a.shape[0],) + a.shape[1:], value, a.dtype)])

    def edges_padded(a, value=0):
        a = padded(a, E_PAD, value)
        last = a[-GROUP:].reshape(TILES, P, *a.shape[1:])
        a[-GROUP:] = last.swapaxes(0, 1).reshape(GROUP, *a.shape[1:])
        return a

    def row(a):
        return np.ascontiguousarray(a).reshape(1, -1)

    arrays = {
        "x": padded(x, N_PAD),
        "src": edges_padded(src),
        "dst": edges_padded(dst, N),
        "ea": edges_padded(edge_attr_64),
        "ew": edges_padded(edge_weight1),
        "W": np.ascontiguousarray(L0_gnn_W),
        "b": row(L0_gnn_b),
        "eps": row(L0_gnn_eps),
        "W1": np.ascontiguousarray(L1_gnn_W1),
        "b1": row(L1_gnn_b1),
        "W2": np.ascontiguousarray(L1_gnn_W2),
        "b2": row(L1_gnn_b2),
    }
    arrays = {f"in_{name}": a for name, a in arrays.items()}
    nc = bacc.Bacc("TRN2", target_bir_lowering=False, num_devices=1)
    args = [nc.dram_tensor(name, a.shape, mybir.dt.from_np(a.dtype), kind="ExternalInput").ap()
            for name, a in arrays.items()]
    out = nc.dram_tensor("out_nodes", (N_PAD, D), F32, kind="ExternalOutput").ap()
    build(nc, *args, out)
    results = run_bass_kernel_spmd(nc, [arrays], core_ids=[0]).results
    return results[0]["out_nodes"][:N]
```
